# Optimizing a Trainium2 kernel written in Bass

```python
import numpy as np
import jax
import jax.numpy as jnp

def _softmax(x, axis=-1):
    return jax.nn.softmax(x, axis=axis)
def _gelu(x):
    return jax.nn.gelu(x, approximate=True)
def _silu(x):
    return jax.nn.silu(x)
def _sigmoid(x):
    return jax.nn.sigmoid(x)
def _layernorm(x, axis=-1, eps=1e-5):
    m = jnp.mean(x, axis=axis, keepdims=True)
    v = jnp.var(x, axis=axis, keepdims=True)
    return (x - m) / jnp.sqrt(v + eps)
def _scatter_add(tgt, idx, src, axis=0):
    return tgt.at[idx].add(src)
def _segment_sum(src, seg, n):
    return jax.ops.segment_sum(src, seg, n)

kernel_name = 'mk_rec_standalone_d1_rec_d869c8'

def setup_inputs(seed: int = 0):
    np.random.seed(seed)
    _w = jnp.asarray
    def _rec_inputs():
        import jax
        import jax.numpy as jnp
        _rk = jax.random.key(seed)
        r_x = -0.000292821 + 1.00034 * jax.random.normal(jax.random.fold_in(_rk, 1), (1024, 64, 32), jnp.float32)
        return r_x
    r_x = _rec_inputs()
    def _L0_rec_setup():
        import jax, jax.numpy as jnp
        import numpy as np
        B, F, E = (2048, 64, 32)
        H1, H2 = (64, 64)

        def _cin_layer(x0, hidden, W, b, n_fields, h_prev):
            Wr = W.reshape(W.shape[0], n_fields, h_prev)
            z = jnp.einsum('ofh,bef,beh->boe', Wr, x0, hidden) + b[:, None]
            return jax.nn.relu(z)
        key = jax.random.key(seed)
        k_x, k_w1, k_b1, k_w2, k_b2 = jax.random.split(key, 5)
        x = jax.random.normal(k_x, (B, F, E), dtype=jnp.float32)
        lim1 = float(np.sqrt(6.0 / (F * F + 2 * H1)))
        W1 = jax.random.uniform(k_w1, (2 * H1, F * F), jnp.float32, -lim1, lim1)
        b1 = jnp.zeros((2 * H1,), jnp.float32)
        lim2 = float(np.sqrt(6.0 / (F * H1 + H2)))
        W2 = jax.random.uniform(k_w2, (H2, F * H1), jnp.float32, -lim2, lim2)
        b2 = jnp.zeros((H2,), jnp.float32)
        return {'x': x, 'W1': W1, 'b1': b1, 'W2': W2, 'b2': b2}
    _L0_rec_all = _L0_rec_setup()
    _L0_rec_in = {k: v for k, v in _L0_rec_all.items() if k in ('W1', 'b1', 'W2', 'b2', )}
    del _L0_rec_all

    return {
        "r_x": r_x,
        "L0_rec_W1": _L0_rec_in["W1"],
        "L0_rec_b1": _L0_rec_in["b1"],
        "L0_rec_W2": _L0_rec_in["W2"],
        "L0_rec_b2": _L0_rec_in["b2"],
    }

def reference(r_x, L0_rec_W1, L0_rec_b1, L0_rec_W2, L0_rec_b2):
    import jax
    import jax.numpy as jnp
    def _L0_rec_ref(x, W1, b1, W2, b2):
        import jax, jax.numpy as jnp
        import numpy as np
        B, F, E = (2048, 64, 32)
        H1, H2 = (64, 64)

        def _cin_layer(x0, hidden, W, b, n_fields, h_prev):
            Wr = W.reshape(W.shape[0], n_fields, h_prev)
            z = jnp.einsum('ofh,bef,beh->boe', Wr, x0, hidden) + b[:, None]
            return jax.nn.relu(z)
        x0 = jnp.transpose(x, (0, 2, 1))
        z1 = _cin_layer(x0, x0, W1, b1, F, F)
        direct1, nxt = (z1[:, :H1, :], z1[:, H1:, :])
        hidden1 = jnp.transpose(nxt, (0, 2, 1))
        z2 = _cin_layer(x0, hidden1, W2, b2, F, H1)
        out = jnp.concatenate([direct1, z2], axis=1)
        return jnp.sum(out, axis=-1)

    y = _L0_rec_ref(r_x, L0_rec_W1, L0_rec_b1, L0_rec_W2, L0_rec_b2)
    return y


_drawn_inputs = setup_inputs


def setup_inputs(seed=0):
    import zlib

    import numpy as np

    out = dict(_drawn_inputs(seed))
    spreads = {'L0_rec_b1': (0.0, 0.1), 'L0_rec_b2': (0.0, 0.1)}
    factors = {}
    for name, (base, spread) in spreads.items():
        noise = np.random.default_rng([zlib.crc32(name.encode()), seed]).standard_normal(out[name].shape)
        drawn = base * np.exp(spread * noise) if base else spread * noise
        out[name] = jnp.asarray(drawn.astype(out[name].dtype))
    for name, factor in factors.items():
        out[name] = (out[name] * factor).astype(out[name].dtype)
    return out
```

```python
import concourse.bass as bass
from concourse import mybir
from contextlib import ExitStack

B, F, E = 1024, 64, 32
H1, H2 = 64, 64
O1 = 2 * H1
N = B * E
CH = 1024
HALF = CH // 2
NCH = N // CH
NB = HALF // E
NA = 4
NROT = 8
L1G = 4
LAG = 6
TRIPLES = L1G * NCH
GRP = 8
P = 128


def cin_program(nc, xT, w1f, w1r, w1d, w2t, b1, b2, y):
    fp32 = mybir.dt.float32
    ALU = mybir.AluOpType
    ACT = mybir.ActivationFunctionType
    AX_X = mybir.AxisListType.X

    ctx = ExitStack()
    with ctx:
        def sb(name, shape):
            return ctx.enter_context(nc.sbuf_tensor(name, shape, fp32))

        def sem(name):
            return ctx.enter_context(nc.semaphore(name))

        x_base = sb("x_base", [P, 2, CH])
        x_fine = sb("x_fine", [P, 2, NA, CH])
        x_coarse = sb("x_coarse", [P, 2, L1G, CH])
        x_late = sb("x_late", [P, 4, CH])
        h_base = sb("h_base", [P, CH])
        h_fine = sb("h_fine", [P, 2, NA, CH])
        prod = sb("prod", [P, 3, NA, CH])
        squares = sb("squares", [P, HALF])
        w1 = sb("w1", [P, L1G * NA, O1])
        w1_diag = sb("w1_diag", [P, O1])
        w2 = sb("w2", [P, NROT * NA, H2])
        b1_sb = sb("b1_sb", [P, 1])
        b2_sb = sb("b2_sb", [P, 1])
        relus = sb("relus", [P, 2, 2, HALF])
        sums = sb("sums", [P, 2, NCH, NB])
        ident = sb("ident", [P, P])
        w1_swapped = prod[:, 1, 0:2, :].rearrange("p a n -> p (a n)").rearrange("p (t o) -> p t o", o=O1)

        z1 = [ctx.enter_context(nc.psum_tensor(f"z1_{s}", [P, 2, HALF], fp32)) for s in range(2)]
        z2 = [ctx.enter_context(nc.psum_tensor(f"z2_{s}", [P, HALF], fp32)) for s in range(2)]
        z_out = [ctx.enter_context(nc.psum_tensor(f"z_out_{s}", [P, 2, P], fp32)) for s in range(2)]
        y_sb = prod[:, 2, 0, :].rearrange("p (g n) -> p g n", g=NCH // GRP)

        base_loaded = [sem(f"base_loaded{s}") for s in range(2)]
        fine_ready = [sem(f"fine_ready{s}") for s in range(2)]
        coarse_ready = [[sem(f"coarse_ready{s}_{k}") for k in range(2)] for s in range(2)]
        late_ready = [sem(f"late_ready{k}") for k in range(2)]
        hfine_ready = [sem(f"hfine_ready{s}") for s in range(2)]
        w1_loaded = sem("w1_loaded")
        w2_loaded = sem("w2_loaded")
        bias_loaded = sem("bias_loaded")
        w1_summed = sem("w1_summed")
        squares_made = sem("squares_made")
        squares_used = sem("squares_used")
        pairs1_made = sem("pairs1_made")
        pairs1_used = sem("pairs1_used")
        pairs2_made = sem("pairs2_made")
        pairs2_used = sem("pairs2_used")
        hidden_made = sem("hidden_made")
        z1_read = sem("z1_read")
        z2_read = sem("z2_read")
        reduced = sem("reduced")
        ident_zero = sem("ident_zero")
        ident_made = sem("ident_made")
        turned = sem("turned")
        y_copied = sem("y_copied")
        y_stored = sem("y_stored")

        block = ctx.enter_context(nc.Block())

        def groups1(c):
            return (c + 1) * L1G

        def groups2(c, k=3):
            return c * 8 + 2 * (k + 1)

        @block.sync
        def _(sp):
            def load_base(n0, s):
                sp.dma_start(x_base[0:F, s, :],
                             xT[:, bass.ds(n0, CH)]).then_inc(base_loaded[s], 16)
                sp.dma_start(x_base[F:P, s, :], xT[:, bass.ds(n0, CH)]).then_inc(base_loaded[s], 16)

            def rotate_fine(s):
                for a in range(NA):
                    for u in range(2):
                        r = 2 * a + u
                        sp.dma_start(x_fine[F * u:F * u + F, s, a, :],
                                     x_base[r:r + F, s, :]).then_inc(fine_ready[s], 16)

            def rotate_coarse(s, k):
                for b in (2 * k + 1, 2 * k + 2):
                    for u in range(2):
                        sp.dma_start(x_coarse[F * u:F * u + F, s, b - 1, :],
                                     x_base[8 * b:8 * b + F, s, :]).then_inc(coarse_ready[s][k], 16)

            def rotate_late(s, k):
                for m in (2 * k, 2 * k + 1):
                    r = 8 * (m + 1)
                    for u in range(2):
                        sp.dma_start(x_late[F * u:F * u + F, m, :],
                                     x_coarse[r:r + F, s, L1G - 1, :]).then_inc(late_ready[k], 16)

            regs = []

            def counts(c, s, i):
                def now(v):
                    if isinstance(v, int):
                        return v
                    r = sp.alloc_register(f"count{s}_{len(regs)}")
                    regs.append(r)
                    sp.reg_mov(r, v)
                    return sp.snap(r)

                uses = i + s
                return {
                    "read2": [now(groups2(c - 2, k)) for k in range(4)],
                    "late_before": now((c - 1) * 64),
                    "fine": now(uses * 128),
                    "coarse": now(uses * 64),
                    "squared": now(c),
                    "base": now(uses * 32 + 32),
                    "read1": now(groups1(c - 1)),
                    "next": (c + 1) * CH,
                }

            def coarse_step(n, s, k):
                sp.wait_ge(pairs2_made, n["read2"][k])
                if k == 1:
                    sp.wait_ge(late_ready[0], n["late_before"])
                    sp.wait_ge(late_ready[1], n["late_before"])
                rotate_coarse(s, k)

            def next_base(n, s):
                sp.wait_ge(fine_ready[1 - s], n["fine"])
                for k in range(2):
                    sp.wait_ge(coarse_ready[1 - s][k], n["coarse"])
                sp.wait_ge(squares_made, n["squared"])
                load_base(n["next"], 1 - s)
                sp.wait_ge(base_loaded[1 - s], n["base"])
                sp.wait_ge(pairs1_made, n["read1"])
                rotate_fine(1 - s)

            def late_step(n, s, first=False):
                sp.wait_ge(coarse_ready[1 - s][1], n["coarse"])
                for k in range(2):
                    if not first:
                        sp.wait_ge(pairs2_made, n["read2"][2 + k])
                    rotate_late(1 - s, k)

            load_base(0, 0)
            sp.wait_ge(base_loaded[0], 32)
            rotate_fine(0)
            rotate_coarse(0, 0)
            rotate_coarse(0, 1)
            load_base(CH, 1)
            sp.wait_ge(base_loaded[1], 32)
            rotate_fine(1)
            rotate_coarse(1, 0)
            rotate_coarse(1, 1)
            second = counts(1, 1, 0)
            next_base(second, 1)
            late_step(second, 1, first=True)

            def step(n, s, more=True):
                coarse_step(n, s, 0)
                coarse_step(n, s, 1)
                if more:
                    next_base(n, s)
                late_step(n, s)

            with sp.Fori(1, NCH // 2 - 1) as i:
                even, odd = counts(i * 2, 0, i), counts(i * 2 + 1, 1, i)
                step(even, 0)
                step(odd, 1)
            step(counts(NCH - 2, 0, NCH // 2 - 1), 0)
            step(counts(NCH - 1, 1, NCH // 2 - 1), 1, more=False)
            late_step(counts(NCH, 0, NCH // 2), 0)

            y_v = y.rearrange("(g c h b) o -> g h c b o", g=NCH // GRP, c=GRP, h=2)
            for g in range(NCH // GRP):
                sp.wait_ge(y_copied, g + 1)
                for h in range(2):
                    sp.dma_start(y_v[g, h], y_sb[:, g, h * O1:h * O1 + O1]).then_inc(y_stored, 16)
            sp.wait_ge(y_stored, 16 * 2 * (NCH // GRP))

        @block.gpsimd
        def _(pool):
            nc.gpsimd.memset(ident[:], 0.0).then_inc(ident_zero, 1)
            pool.wait_ge(ident_zero, 1)
            nc.gpsimd.affine_select(out=ident[:], in_=ident[:], compare_op=ALU.not_equal, fill=1.0, base=0,
                                    pattern=[[-1, P]], channel_multiplier=1).then_inc(ident_made, 1)

        @block.vector
        def _(dve):
            dve.wait_ge(w1_loaded, 64)
            last = L1G * NA - NA
            for lo, t0, t1 in ((0, 0, last), (0, last + 1, L1G * NA)):
                nc.vector.tensor_tensor(w1[lo:P, t0:t1, :], w1[lo:P, t0:t1, :], w1_swapped[lo:P, t0:t1, :],
                                        ALU.add).then_inc(w1_summed, 1)
            nc.vector.tensor_tensor(w1[F:P, last, :], w1[F:P, last, :], w1_swapped[F:P, last, :],
                                    ALU.add).then_inc(w1_summed, 1)
            dve.wait_ge(w1_summed, 3)

            def layer1(t, j, i):
                s, q = (j // 4) % 2, j % 4
                if q == 0:
                    dve.wait_ge(fine_ready[s], i * 128 + 128)
                if q % 2 == 0:
                    dve.wait_ge(coarse_ready[s][q // 2], i * 64 + 64)
                if not isinstance(t, int) or t > 0:
                    dve.wait_ge(pairs1_used, t)
                nc.vector.tensor_tensor(prod[:, 0], x_fine[:, s], x_coarse[:, s, q:q + 1, :].to_broadcast([P, NA, CH]),
                                        ALU.mult).then_inc(pairs1_made, 1)

            def layer2(t, j, i):
                u = (j - LAG) % 8
                s, k = u // 4, u % 4
                if k == 0:
                    dve.wait_ge(hfine_ready[s], i * 128 + 128)
                if k >= 2:
                    dve.wait_ge(late_ready[k - 2], (i * 2 + s) * 64 + 64)
                for m in range(2):
                    if not isinstance(t, int) or t > LAG:
                        dve.wait_ge(pairs2_used, (t - LAG) * 2 + m - 1)
                    coarse = x_coarse[:, s, 2 * k + m:2 * k + m + 1, :] if k < 2 else x_late[:, 2 * k + m - 4:2 * k + m - 3, :]
                    nc.vector.tensor_tensor(prod[:, 1 + m], h_fine[:, s], coarse.to_broadcast([P, NA, CH]),
                                            ALU.mult).then_inc(pairs2_made, 1)

            def reduce(c, s):
                dve.wait_ge(z2_read, c + 1)
                nc.vector.reduce_sum(sums[:, :, bass.ds(c, 1), :].rearrange("p k c b -> p k (c b)"),
                                     relus[:, s].rearrange("p k (b e) -> p k b e", e=E),
                                     AX_X).then_inc(reduced, 1)

            for t in range(8):
                layer1(t, t, 0)
                if t >= LAG:
                    layer2(t, t, 0)
            with dve.Fori(1, TRIPLES // 8) as i:
                for j in range(8):
                    layer1(i * 8 + j, j, i)
                    layer2(i * 8 + j, j, i if j >= LAG else i - 1)
                    if j % 4 == 2:
                        reduce(i * 2 + j // 4 - 2, j // 4)
            for j in range(LAG):
                layer2(TRIPLES + j, j, NCH // 2 - 1)
                if j == 2:
                    reduce(NCH - 2, 0)
            reduce(NCH - 1, 1)
            for g in range(NCH // GRP):
                dve.wait_ge(turned, g + 1)
                nc.vector.tensor_copy(y_sb[:, g, :].rearrange("p (h k o) -> p h k o", h=2, k=2),
                                      z_out[g % 2][:, :, :].rearrange("p k (h o) -> p h k o", h=2)).then_inc(y_copied, 1)

        @block.tensor
        def _(pe):
            pe.wait_ge(w1_summed, 3)
            pe.wait_ge(w1_loaded, 64)
            pe.wait_ge(w2_loaded, 16)

            def layer1(t, j, c, fresh):
                s, q = (j // 4) % 2, j % 4
                if q == 0:
                    if not fresh:
                        pe.wait_ge(z1_read, c - 1)
                    pe.wait_ge(squares_made, c + 1)
                    for h in range(2):
                        mm = nc.tensor.matmul(z1[s][:, h, :], w1_diag[F * h:F * h + F, :],
                                              squares[F * h:F * h + F, :], start=True, stop=False)
                    mm.then_inc(squares_used, 1)
                pe.wait_ge(pairs1_made, t + 1)
                for a in range(NA):
                    for h in range(2):
                        mm = nc.tensor.matmul(z1[s][:, h, :], w1[:, NA * q + a, :],
                                              prod[:, 0, a, h * HALF:(h + 1) * HALF],
                                              start=False, stop=(q == L1G - 1 and a == NA - 1))
                mm.then_inc(pairs1_used, 1)

            def layer2(t, j, c, fresh):
                u = (j - LAG) % 8
                s, k = u // 4, u % 4
                if k == 0 and not fresh:
                    pe.wait_ge(z2_read, c - 1)
                for m in range(2):
                    b = (2 * k + m + 1) % NROT
                    pe.wait_ge(pairs2_made, (t - LAG) * 2 + m + 1)
                    for a in range(NA):
                        for h in range(2):
                            mm = nc.tensor.matmul(z2[s][F * h:F * h + F, :], w2[:, NA * b + a, :],
                                                  prod[:, 1 + m, a, h * HALF:(h + 1) * HALF],
                                                  start=(k == 0 and m == 0 and a == 0),
                                                  stop=(k == 3 and m == 1 and a == NA - 1))
                    mm.then_inc(pairs2_used, 1)

            for t in range(16):
                layer1(t, t % 8, t // 4, t // 4 < 2)
                if t >= LAG:
                    layer2(t, t % 8, (t - LAG) // 4, (t - LAG) // 4 < 2)
            with pe.Fori(2, TRIPLES // 8) as i:
                for j in range(8):
                    layer1(i * 8 + j, j, i * 2 + j // 4, False)
                    layer2(i * 8 + j, j, i * 2 + (j - LAG) // 4, False)
            for j in range(LAG):
                layer2(TRIPLES + j, j, NCH + (j - LAG) // 4, False)

            pe.wait_ge(ident_made, 1)
            for g in range(NCH // GRP):
                pe.wait_ge(reduced, GRP * (g + 1))
                if g >= 2:
                    pe.wait_ge(y_copied, g - 1)
                for k in range(2):
                    mm = nc.tensor.transpose(z_out[g % 2][:, k, :], sums[:, k, GRP * g:GRP * g + GRP, :].rearrange("p c b -> p (c b)"),
                                             ident[:])
                mm.then_inc(turned, 1)

        @block.scalar
        def _(act):
            act.dma_start(w1[:], w1f).then_inc(w1_loaded, 16)
            act.dma_start(w1_swapped, w1r).then_inc(w1_loaded, 16)
            for h in range(2):
                act.dma_start(w1_diag[F * h:F * h + F, :], w1d).then_inc(w1_loaded, 16)
            act.dma_start(b1_sb[:], b1).then_inc(bias_loaded, 16)
            for h in range(2):
                act.dma_start(b2_sb[F * h:F * h + F, :], b2).then_inc(bias_loaded, 16)
            act.dma_start(w2[:], w2t).then_inc(w2_loaded, 16)
            act.wait_ge(bias_loaded, 48)

            def square(s, c, i):
                act.wait_ge(base_loaded[s], i * 32 + 32)
                if not isinstance(c, int) or c > 0:
                    act.wait_ge(squares_used, c)
                for h in range(2):
                    sq = nc.scalar.activation(squares[F * h:F * h + F, :],
                                              x_base[F * h:F * h + F, s, h * HALF:(h + 1) * HALF], ACT.Square)
                sq.then_inc(squares_made, 1)

            def read_z1(s, c, i, fresh):
                act.wait_ge(pairs1_used, groups1(c))
                if not isinstance(c, int) or c > 0:
                    act.wait_ge(hfine_ready[1 - s], (i + s) * 128)
                z1_rows = z1[s][H1:O1].rearrange("p h n -> p (h n)")
                for h in range(2):
                    nc.scalar.activation(h_base[F * h:F * h + F, :], z1_rows, ACT.Relu,
                                         bias=b1_sb[H1:O1, :]).then_inc(hidden_made, 1)
                act.wait_ge(hidden_made, c * 2 + 2)
                if not fresh:
                    act.wait_ge(pairs2_made, groups2(c - 2))
                for a in range(NA):
                    for u in range(2):
                        r = 2 * a + u
                        act.dma_start(h_fine[F * u:F * u + F, s, a, :], h_base[r:r + F, :]).then_inc(hfine_ready[s], 16)
                if not fresh:
                    act.wait_ge(reduced, c - 1)
                for h in range(2):
                    rd = nc.scalar.activation(relus[F * h:F * h + F, s, 0, :], z1[s][0:H1, h, :], ACT.Relu,
                                              bias=b1_sb[0:H1, :])
                rd.then_inc(z1_read, 1)

            def read_z2(s, c):
                act.wait_ge(pairs2_used, groups2(c))
                nc.scalar.activation(relus[:, s, 1, :], z2[s][:, :], ACT.Relu, bias=b2_sb[:]).then_inc(z2_read, 1)

            square(0, 0, 0)
            square(1, 1, 0)
            read_z1(0, 0, 0, True)
            square(0, 2, 1)
            read_z1(1, 1, 0, True)
            with act.Fori(1, NCH // 2 - 1) as i:
                square(1, i * 2 + 1, i)
                read_z2(0, i * 2 - 2)
                read_z1(0, i * 2, i, False)
                square(0, i * 2 + 2, i + 1)
                read_z2(1, i * 2 - 1)
                read_z1(1, i * 2 + 1, i, False)
            square(1, NCH - 1, NCH // 2 - 1)
            read_z2(0, NCH - 4)
            read_z1(0, NCH - 2, NCH // 2 - 1, False)
            read_z2(1, NCH - 3)
            read_z1(1, NCH - 1, NCH // 2 - 1, False)
            read_z2(0, NCH - 2)
            read_z2(1, NCH - 1)


def kernel(r_x, L0_rec_W1, L0_rec_b1, L0_rec_W2, L0_rec_b2):
    import numpy as np
    import concourse.bacc as bacc
    from concourse.bass_utils import run_bass_kernel_spmd

    x, W1, W2 = (np.asarray(a) for a in (r_x, L0_rec_W1, L0_rec_W2))
    W1 = W1.reshape(O1, F, F)
    W2 = W2.reshape(H2, F, H1)
    p = np.arange(P)
    row, upper = p % F, p // F
    coarse = (row[:, None] + 8 * np.arange(NROT)[None, :]) % F
    fine = (row[:, None] + 2 * np.arange(NA)[None, :] + upper[:, None]) % F
    c1 = np.repeat(coarse[:, 1:L1G + 1], NA, axis=1)
    f1 = np.tile(fine, (1, L1G))
    c2 = np.repeat(coarse, NA, axis=1)
    f2 = np.tile(fine, (1, NROT))
    rows = np.arange(F)
    arrays = {
        "xT": np.ascontiguousarray(x.transpose(1, 0, 2).reshape(F, N)),
        "w1f": np.ascontiguousarray(W1[:, f1, c1].transpose(1, 2, 0)),
        "w1r": np.ascontiguousarray(W1[:, c1, f1].transpose(1, 2, 0)),
        "w1d": np.ascontiguousarray(W1[:, rows, rows].transpose(1, 0)),
        "w2t": np.ascontiguousarray(W2[:, c2, f2].transpose(1, 2, 0)),
        "b1": np.ascontiguousarray(np.asarray(L0_rec_b1).reshape(O1, 1)),
        "b2": np.ascontiguousarray(np.asarray(L0_rec_b2).reshape(H2, 1)),
    }
    nc = bacc.Bacc("TRN2", target_bir_lowering=False, num_devices=1)
    args = [nc.dram_tensor(name, a.shape, mybir.dt.from_np(a.dtype), kind="ExternalInput").ap()
            for name, a in arrays.items()]
    args.append(nc.dram_tensor("y", (B, O1), mybir.dt.float32, kind="ExternalOutput").ap())
    cin_program(nc, *args)
    return run_bass_kernel_spmd(nc, [arrays], core_ids=[0]).results[0]["y"]
```

```python
import concourse.bass as bass
from concourse import mybir
from contextlib import ExitStack

B, F, E = 1024, 64, 32
H1, H2 = 64, 64
O1 = 2 * H1
N = B * E
CH = 1024
HALF = CH // 2
NCH = N // CH
NB = HALF // E
NA = 4
NROT = 8
L1G = 4
L2G = 8
SLOTS = 4
GRP = 8
NSPLIT = 2
NFULL = NA - NSPLIT
HFIRST = 5
P = 128


def cin_program(nc, xT, w1f, w1r, w1d, w2t, b1, b2, y):
    fp32 = mybir.dt.float32
    fp32r = mybir.dt.float32r
    ALU = mybir.AluOpType
    ACT = mybir.ActivationFunctionType
    AX_X = mybir.AxisListType.X

    ctx = ExitStack()
    with ctx:
        def sb(name, shape, dtype=fp32):
            return ctx.enter_context(nc.sbuf_tensor(name, shape, dtype))

        def sem(name):
            return ctx.enter_context(nc.semaphore(name))

        x_base = sb("x_base", [P, CH])
        x_fine = sb("x_fine", [P, NA, CH])
        x_coarse = sb("x_coarse", [P, 2, L1G, CH])
        x_late = sb("x_late", [P, 2, CH])
        h_base = sb("h_base", [P, CH])
        h_fine = sb("h_fine", [P, NA, CH])
        prod = sb("prod", [P, SLOTS, NA, CH])
        prod_hi = sb("prod_hi", [P, 2, NSPLIT, CH], fp32r)
        prod_lo = sb("prod_lo", [P, 2, NSPLIT, CH], fp32r)
        squares = sb("squares", [P, HALF])
        w1 = sb("w1", [P, L1G, NFULL, O1])
        w1_hi = sb("w1_hi", [P, L1G, NSPLIT, O1], fp32r)
        w1_lo = sb("w1_lo", [P, L1G, NSPLIT, O1], fp32r)
        w1_diag = sb("w1_diag", [P, O1])
        w2 = sb("w2", [P, NROT * NA, H2])
        b1_sb = sb("b1_sb", [P, 1])
        b2_sb = sb("b2_sb", [P, 1])
        relus = sb("relus", [P, 2, HALF])
        sums = sb("sums", [P, 2, NCH + 1, NB])
        ident = sb("ident", [P, P])
        w1_swapped = h_fine[:, 0:2, :].rearrange("p a n -> p (a n)").rearrange("p (q a o) -> p q a o", q=L1G, a=NA)
        w1_split = h_fine[:, 2, :].rearrange("p (q a o) -> p q a o", q=L1G, a=NSPLIT)
        y_sb = x_coarse[:, 0, 0, :].rearrange("p (g n) -> p g n", g=NCH // GRP)

        coarse_ps = ctx.enter_context(nc.psum_tensor("coarse_ps", [P, 2, CH], fp32))
        z1 = ctx.enter_context(nc.psum_tensor("z1", [P, 2, HALF], fp32))
        z2 = ctx.enter_context(nc.psum_tensor("z2", [P, HALF], fp32))
        z_out = ctx.enter_context(nc.psum_tensor("z_out", [P, 2, P], fp32))

        base_loaded = sem("base_loaded")
        fine_ready = sem("fine_ready")
        first_fine = [sem(f"first_fine{a}") for a in range(NA)]
        coarse_ready = [[sem(f"coarse_ready{s}_{k}") for k in range(L1G)] for s in range(2)]
        late_ready = [sem(f"late_ready{s}") for s in range(2)]
        hfine_ready = sem("hfine_ready")
        coarse1_copied = sem("coarse1_copied")
        coarse2_copied = sem("coarse2_copied")
        hi_made = sem("hi_made")
        lo_made = sem("lo_made")
        w1_loaded = [sem(f"w1_loaded{q}") for q in range(L1G)]
        diag_loaded = sem("diag_loaded")
        w2_loaded = sem("w2_loaded")
        bias_loaded = sem("bias_loaded")
        w1_summed = sem("w1_summed")
        w1_hi_made = sem("w1_hi_made")
        w1_lo_made = sem("w1_lo_made")
        squares_made = sem("squares_made")
        squares_used = sem("squares_used")
        pairs1_made = sem("pairs1_made")
        first_pairs = sem("first_pairs")
        pairs1_used = sem("pairs1_used")
        pairs2_made = sem("pairs2_made")
        pairs2_used = sem("pairs2_used")
        hidden_made = sem("hidden_made")
        z1_read = sem("z1_read")
        z2_read = sem("z2_read")
        reduced = sem("reduced")
        ident_zero = sem("ident_zero")
        ident_made = sem("ident_made")
        turned = sem("turned")
        y_copied = sem("y_copied")
        y_stored = sem("y_stored")

        block = ctx.enter_context(nc.Block())

        def groups1(c, q=L1G - 1):
            return c * L1G + (q + 1)

        def groups2(c, g=L2G - 1):
            return c * L2G + (g + 1)

        @block.sync
        def _(sp):
            def load_base(n0):
                for u in range(2):
                    sp.dma_start(x_base[F * u:F * u + F, :], xT[:, bass.ds(n0, CH)]).then_inc(base_loaded, 16)

            def rotate_fine(ready=(fine_ready,) * NA):
                for a in range(NA):
                    for u in range(2):
                        r = 2 * a + u
                        sp.dma_start(x_fine[F * u:F * u + F, a, :], x_base[r:r + F, :]).then_inc(ready[a], 16)

            def rotate_coarse(s, b):
                for u in range(2):
                    sp.dma_start(x_coarse[F * u:F * u + F, s, b - 1, :],
                                 x_base[8 * b:8 * b + F, :]).then_inc(coarse_ready[s][b - 1], 16)

            def rotate_late(s, m):
                r = 8 * (m + 1)
                for u in range(2):
                    sp.dma_start(x_late[F * u:F * u + F, m % 2, :],
                                 x_coarse[r:r + F, s, L1G - 1, :]).then_inc(late_ready[m % 2], 16)

            regs = []

            def counts(c, s, i):
                def now(v):
                    if isinstance(v, int):
                        return v
                    r = sp.alloc_register(f"count{s}_{len(regs)}")
                    regs.append(r)
                    sp.reg_mov(r, v)
                    return sp.snap(r)

                return {
                    "base": now((c + 1) * 32),
                    "read1": now(groups1(c - 1)),
                    "copied": [now(groups2(c - 2, g)) for g in range(2, L2G)],
                    "late": now((c - 1) * 64),
                    "source": now((i + s) * 32),
                    "fine": now(c * 128),
                    "coarse": now(i * 32 + 32),
                    "squared": now(c + 1),
                    "next": (c + 1) * CH,
                }

            def fine_step(n):
                sp.wait_ge(base_loaded, n["base"])
                sp.wait_ge(pairs1_made, n["read1"])
                rotate_fine()

            def late_second(n, s):
                for m in (2, 3):
                    sp.wait_ge(coarse2_copied, n["copied"][L1G + m - 4])
                    rotate_late(s, m)

            def late_first(n, s):
                sp.wait_ge(coarse_ready[1 - s][L1G - 1], n["source"])
                for m in (0, 1):
                    sp.wait_ge(coarse2_copied, n["copied"][L1G + m])
                    rotate_late(1 - s, m)

            def next_base(n, s, first=False):
                if first:
                    for a in range(NA):
                        sp.wait_ge(first_fine[a], 32)
                else:
                    sp.wait_ge(fine_ready, n["fine"])
                for b in range(L1G):
                    sp.wait_ge(coarse_ready[s][b], n["coarse"])
                sp.wait_ge(squares_made, n["squared"])
                load_base(n["next"])

            def step(n, s, more=True):
                fine_step(n)
                sp.wait_ge(coarse2_copied, n["copied"][0])
                for b in range(1, L1G):
                    rotate_coarse(s, b)
                late_second(n, s)
                for m in range(2):
                    sp.wait_ge(late_ready[m], n["late"])
                rotate_coarse(s, L1G)
                late_first(n, s)
                if more:
                    next_base(n, s)

            load_base(0)
            sp.wait_ge(base_loaded, 32)
            rotate_coarse(0, 1)
            rotate_fine(ready=first_fine)
            for b in range(2, L1G + 1):
                rotate_coarse(0, b)
            next_base(counts(0, 0, 0), 0, first=True)
            second = counts(1, 1, 0)
            sp.wait_ge(base_loaded, second["base"])
            for b in range(1, L1G + 1):
                rotate_coarse(1, b)
            sp.wait_ge(coarse_ready[0][L1G - 1], second["source"])
            for m in (0, 1):
                rotate_late(0, m)
            fine_step(second)
            next_base(second, 1)
            with sp.Fori(1, NCH // 2 - 1) as i:
                even, odd = counts(i * 2, 0, i), counts(i * 2 + 1, 1, i)
                step(even, 0)
                step(odd, 1)
            step(counts(NCH - 2, 0, NCH // 2 - 1), 0)
            step(counts(NCH - 1, 1, NCH // 2 - 1), 1, more=False)
            beyond = counts(NCH, 0, NCH // 2)
            late_second(beyond, 0)
            late_first(beyond, 0)
            late_second(counts(NCH + 1, 1, NCH // 2), 1)

            y_v = y.rearrange("(g c h b) o -> g h c b o", g=NCH // GRP, c=GRP, h=2)
            for g in range(NCH // GRP):
                sp.wait_ge(y_copied, g + 1)
                for h in range(2):
                    sp.dma_start(y_v[g, h], y_sb[:, g, h * O1:h * O1 + O1]).then_inc(y_stored, 16)
            sp.wait_ge(y_stored, 16 * 2 * (NCH // GRP))

        @block.gpsimd
        def _(pool):
            nc.gpsimd.memset(ident[:], 0.0).then_inc(ident_zero, 1)
            pool.wait_ge(ident_zero, 1)
            nc.gpsimd.affine_select(out=ident[:], in_=ident[:], compare_op=ALU.not_equal, fill=1.0, base=0,
                                    pattern=[[-1, P]], channel_multiplier=1).then_inc(ident_made, 1)

            def rest(c):
                for q in range(L1G):
                    pool.wait_ge(hi_made, groups1(c, q))
                    nc.gpsimd.tensor_tensor(prod_lo[:, q % 2], prod[:, q, NFULL:NA],
                                            prod_hi[:, q % 2].bitcast(fp32), ALU.subtract).then_inc(lo_made, 1)

            with pool.Fori(0, NCH) as c:
                rest(c)

        @block.vector
        def _(dve):
            def sum_weights(q):
                dve.wait_ge(w1_loaded[q], 48)
                if q == L1G - 1:
                    nc.vector.tensor_tensor(w1[F:P, q, 0, :], w1[F:P, q, 0, :], w1_swapped[F:P, q, 0, :],
                                            ALU.add).then_inc(w1_summed, 1)
                    nc.vector.tensor_tensor(w1[:, q, 1:, :], w1[:, q, 1:, :], w1_swapped[:, q, 1:NFULL, :],
                                            ALU.add).then_inc(w1_summed, 1)
                else:
                    nc.vector.tensor_tensor(w1[:, q], w1[:, q], w1_swapped[:, q, 0:NFULL, :],
                                            ALU.add).then_inc(w1_summed, 1)
                nc.vector.tensor_tensor(w1_split[:, q], w1_split[:, q], w1_swapped[:, q, NFULL:NA, :],
                                        ALU.add).then_inc(w1_summed, 1)

            def split_weights(q):
                dve.wait_ge(w1_hi_made, q + 1)
                nc.vector.tensor_tensor(w1_lo[:, q], w1_split[:, q], w1_hi[:, q].bitcast(fp32),
                                        ALU.subtract).then_inc(w1_lo_made, 1)

            def copied(slot):
                return coarse_ps[:, slot:slot + 1, :].to_broadcast([P, NA, CH])

            def layer1(c):
                for q in range(L1G):
                    if q == 0 and not (isinstance(c, int) and c == 0):
                        dve.wait_ge(fine_ready, c * 128)
                    dve.wait_ge(coarse1_copied, groups1(c, q))
                    if not isinstance(c, int) or c > 1:
                        dve.wait_ge(pairs2_used, groups2(c - 2, L2G - SLOTS + q))
                    elif c == 1:
                        dve.wait_ge(pairs1_used, groups1(0, q))
                    if isinstance(c, int) and c == 0 and q == 0:
                        for a in range(NA):
                            dve.wait_ge(first_fine[a], 32)
                            nc.vector.tensor_tensor(prod[:, q, a], x_fine[:, a], coarse_ps[:, q % 2],
                                                    ALU.mult).then_inc(pairs1_made if a == NA - 1 else first_pairs, 1)
                    else:
                        nc.vector.tensor_tensor(prod[:, q], x_fine[:, :], copied(q % 2),
                                                ALU.mult).then_inc(pairs1_made, 1)
                    if isinstance(c, int) and c == 0:
                        if q > 0:
                            sum_weights(q)
                        split_weights(q)

            def layer2(c, reduces=True, last=False):
                for g in range(L2G):
                    if g == 0:
                        dve.wait_ge(hfine_ready, (c + 1) * 128)
                    dve.wait_ge(coarse2_copied, groups2(c, g))
                    if g >= SLOTS:
                        dve.wait_ge(pairs2_used, groups2(c, g - SLOTS))
                    elif last:
                        dve.wait_ge(pairs2_used, groups2(c - 1, g + SLOTS))
                    else:
                        dve.wait_ge(pairs1_used, groups1(c + 1, g))
                    nc.vector.tensor_tensor(prod[:, g % SLOTS], x_fine[:, :] if last else h_fine[:, :],
                                            copied(g % 2), ALU.mult).then_inc(pairs2_made, 1)
                    if g == 1 and reduces:
                        reduce(c)

            def reduce(c):
                dve.wait_ge(z2_read, c)
                nc.vector.reduce_sum(sums[:, :, bass.ds(c, 1), :].rearrange("p k c b -> p k (c b)"),
                                     relus[:, :, :].rearrange("p k (b e) -> p k b e", e=E),
                                     AX_X).then_inc(reduced, 1)

            def reduce_one(c, k):
                nc.vector.reduce_sum(sums[:, k, c, :], relus[:, k, :].rearrange("p (b e) -> p b e", e=E),
                                     AX_X).then_inc(reduced, 1)

            sum_weights(0)
            layer1(0)
            layer1(1)
            layer2(0, reduces=False)
            dve.wait_ge(z1_read, 1)
            reduce_one(0, 0)
            with dve.Fori(1, NCH // 2) as i:
                layer1(i * 2)
                layer2(i * 2 - 1)
                layer1(i * 2 + 1)
                layer2(i * 2)
            layer2(NCH - 1, last=True)
            dve.wait_ge(z2_read, NCH)
            reduce_one(NCH, 1)

        @block.tensor
        def _(pe):
            pe.wait_ge(diag_loaded, 32)

            def layer1(c):
                if not isinstance(c, int) or c > 0:
                    pe.wait_ge(z1_read, c)
                pe.wait_ge(squares_made, c + 1)
                for h in range(2):
                    mm = nc.tensor.matmul(z1[:, h, :], w1_diag[F * h:F * h + F, :],
                                          squares[F * h:F * h + F, :], start=True, stop=False)
                mm.then_inc(squares_used, 1)
                for q in range(L1G):
                    first = isinstance(c, int) and c == 0
                    if first:
                        pe.wait_ge(w1_summed, 2 * (q + 1) + q // (L1G - 1))
                    if not (first and q == 0):
                        pe.wait_ge(pairs1_made, groups1(c, q))
                    for a in range(NFULL):
                        if first and q == 0:
                            pe.wait_ge(first_pairs, a + 1)
                        for h in range(2):
                            nc.tensor.matmul(z1[:, h, :], w1[:, q, a, :],
                                             prod[:, q, a, h * HALF:(h + 1) * HALF], start=False, stop=False)
                    if first:
                        pe.wait_ge(w1_lo_made, q + 1)
                    pe.wait_ge(lo_made, groups1(c, q))
                    for a in range(NSPLIT):
                        for h in range(2):
                            for w, p in ((w1_hi, prod_hi), (w1_lo, prod_hi), (w1_hi, prod_lo)):
                                mm = nc.tensor.matmul(z1[:, h, :], w[:, q, a, :],
                                                      p[:, q % 2, a, h * HALF:(h + 1) * HALF], start=False,
                                                      stop=(q == L1G - 1 and a == NSPLIT - 1 and p is prod_lo))
                    mm.then_inc(pairs1_used, 1)

            def layer2(c, between=None):
                if not isinstance(c, int) or c > 0:
                    pe.wait_ge(z2_read, c)
                for g in range(L2G):
                    b = (g + 1) % NROT
                    pe.wait_ge(pairs2_made, groups2(c, g))
                    for a in range(NA):
                        for h in range(2):
                            mm = nc.tensor.matmul(z2[F * h:F * h + F, :], w2[:, NA * b + a, :],
                                                  prod[:, g % SLOTS, a, h * HALF:(h + 1) * HALF],
                                                  start=(g == 0 and a == 0), stop=(g == L2G - 1 and a == NA - 1))
                    mm.then_inc(pairs2_used, 1)
                    if between and g == 2:
                        between()

            pe.wait_ge(ident_made, 1)

            def turn(g):
                pe.wait_ge(reduced, GRP * (g + 1) + 1)
                if g >= 1:
                    pe.wait_ge(y_copied, g)
                for k in range(2):
                    mm = nc.tensor.transpose(z_out[:, k, :],
                                             sums[:, k, GRP * g + k:GRP * g + k + GRP, :].rearrange("p c b -> p (c b)"),
                                             ident[:])
                mm.then_inc(turned, 1)

            def turn_all_but_last():
                for g in range(NCH // GRP - 1):
                    turn(g)

            layer1(0)
            layer1(1)
            pe.wait_ge(w2_loaded, 16)
            layer2(0)
            with pe.Fori(1, NCH // 2) as i:
                layer1(i * 2)
                layer2(i * 2 - 1)
                layer1(i * 2 + 1)
                layer2(i * 2)
            layer2(NCH - 1, between=turn_all_but_last)
            turn(NCH // GRP - 1)

        @block.scalar
        def _(act):
            def load_w1(q):
                act.dma_start(w1[:, q], w1f[:, q, 0:NFULL, :]).then_inc(w1_loaded[q], 16)
                act.dma_start(w1_split[:, q], w1f[:, q, NFULL:NA, :]).then_inc(w1_loaded[q], 16)
                act.dma_start(w1_swapped[:, q], w1r[:, q]).then_inc(w1_loaded[q], 16)

            def round_w1(q):
                act.wait_ge(w1_summed, 2 * (q + 1) + q // (L1G - 1))
                nc.scalar.activation(w1_hi[:, q], w1_split[:, q], ACT.Copy).then_inc(w1_hi_made, 1)

            load_w1(0)
            for h in range(2):
                act.dma_start(w1_diag[F * h:F * h + F, :], w1d).then_inc(diag_loaded, 16)
            act.dma_start(b1_sb[:], b1).then_inc(bias_loaded, 16)
            for h in range(2):
                act.dma_start(b2_sb[F * h:F * h + F, :], b2).then_inc(bias_loaded, 16)

            def square(c):
                act.wait_ge(base_loaded, (c + 1) * 32)
                if not isinstance(c, int) or c > 0:
                    act.wait_ge(squares_used, c)
                for h in range(2):
                    sq = nc.scalar.activation(squares[F * h:F * h + F, :],
                                              x_base[F * h:F * h + F, h * HALF:(h + 1) * HALF], ACT.Square)
                sq.then_inc(squares_made, 1)

            def copy1(c, s, i, q):
                act.wait_ge(coarse_ready[s][q], i * 32 + 32)
                if q >= 2:
                    act.wait_ge(pairs1_made, groups1(c, q - 2))
                elif not isinstance(c, int) or c > 1:
                    act.wait_ge(pairs2_made, groups2(c - 2, L2G - 2 + q))
                elif c == 1:
                    act.wait_ge(pairs1_made, groups1(0, L1G - 2 + q))
                nc.scalar.activation(coarse_ps[:, q % 2, :], x_coarse[:, s, q, :], ACT.Copy).then_inc(coarse1_copied, 1)

            def copy2(c, s, g, last=False):
                m = g - L1G
                if m >= 0:
                    act.wait_ge(late_ready[m % 2], c * 64 + 32 * (m // 2 + 1))
                if g >= 2:
                    act.wait_ge(pairs2_made, groups2(c, g - 2))
                elif last:
                    act.wait_ge(pairs2_made, groups2(c - 1, L2G - 2 + g))
                else:
                    act.wait_ge(pairs1_made, groups1(c + 1, L1G - 2 + g))
                source = x_coarse[:, s, g, :] if m < 0 else x_late[:, m % 2, :]
                nc.scalar.activation(coarse_ps[:, g % 2, :], source, ACT.Copy).then_inc(coarse2_copied, 1)

            def round_high(c, q):
                act.wait_ge(pairs1_made, groups1(c, q))
                if q >= 2:
                    act.wait_ge(pairs1_used, groups1(c, q - 2))
                elif not isinstance(c, int) or c > 0:
                    act.wait_ge(pairs1_used, groups1(c - 1, q + 2))
                nc.scalar.activation(prod_hi[:, q % 2], prod[:, q, NFULL:NA], ACT.Copy).then_inc(hi_made, 1)

            def read_z1(c):
                act.wait_ge(pairs1_used, groups1(c))
                if not isinstance(c, int) or c > 0:
                    act.wait_ge(hfine_ready, c * 128)
                z1_rows = z1[H1:O1].rearrange("p h n -> p (h n)")
                for h in range(2):
                    nc.scalar.activation(h_base[F * h:F * h + F, :], z1_rows, ACT.Relu,
                                         bias=b1_sb[H1:O1, :]).then_inc(hidden_made, 1)
                if not isinstance(c, int) or c > 0:
                    act.wait_ge(reduced, c)
                for h in range(2):
                    rd = nc.scalar.activation(relus[F * h:F * h + F, 0, :], z1[0:H1, h, :], ACT.Relu,
                                              bias=b1_sb[0:H1, :])
                rd.then_inc(z1_read, 1)

            def rotate_hidden(c, to, first=2 * NA):
                act.wait_ge(hidden_made, c * 2 + 2)
                if isinstance(c, int) and c == NCH - 1:
                    act.wait_ge(pairs1_made, groups1(c))
                elif not isinstance(c, int) or c > 0:
                    act.wait_ge(pairs2_made, groups2(c - 1))
                else:
                    act.wait_ge(w1_lo_made, L1G)
                rotate_hidden_rows(to, 0, first)

            def rotate_hidden_rows(to, start, end):
                for r in range(start, end):
                    a, u = r // 2, r % 2
                    act.dma_start(to[F * u:F * u + F, a, :], h_base[r:r + F, :]).then_inc(hfine_ready, 16)

            def read_z2(c):
                act.wait_ge(pairs2_used, groups2(c))
                if not isinstance(c, int) or c > 0:
                    act.wait_ge(reduced, c + 1)
                nc.scalar.activation(relus[:, 1, :], z2[:, :], ACT.Relu, bias=b2_sb[:]).then_inc(z2_read, 1)

            def step(c, s, i, more=True):
                copy1(c, s, i, 0)
                copy1(c, s, i, 1)
                rotate_hidden(c - 1, h_fine, HFIRST)
                round_high(c, 0)
                copy1(c, s, i, 2)
                rotate_hidden_rows(h_fine, HFIRST, 2 * NA)
                round_high(c, 1)
                copy1(c, s, i, 3)
                if not isinstance(c, int) or c > 1:
                    read_z2(c - 2)
                copy2(c - 1, 1 - s, 0)
                round_high(c, 2)
                copy2(c - 1, 1 - s, 1)
                round_high(c, 3)
                copy2(c - 1, 1 - s, 2)
                copy2(c - 1, 1 - s, 3)
                read_z1(c)
                if more:
                    square(c + 1)
                for g in range(L1G, L2G):
                    copy2(c - 1, 1 - s, g)

            copy1(0, 0, 0, 0)
            square(0)
            round_w1(0)
            act.wait_ge(first_fine[0], 32)
            load_w1(1)
            act.wait_ge(first_fine[NA - 1], 32)
            load_w1(2)
            load_w1(3)
            copy1(0, 0, 0, 1)
            round_high(0, 0)
            copy1(0, 0, 0, 2)
            round_w1(1)
            round_high(0, 1)
            copy1(0, 0, 0, 3)
            round_w1(2)
            round_high(0, 2)
            round_w1(3)
            round_high(0, 3)
            square(1)
            act.wait_ge(bias_loaded, 48)
            act.dma_start(w2[:], w2t).then_inc(w2_loaded, 16)
            copy1(1, 1, 0, 0)
            copy1(1, 1, 0, 1)
            read_z1(0)
            rotate_hidden(0, h_fine)
            copy1(1, 1, 0, 2)
            round_high(1, 0)
            copy1(1, 1, 0, 3)
            round_high(1, 1)
            copy2(0, 0, 0)
            round_high(1, 2)
            copy2(0, 0, 1)
            round_high(1, 3)
            copy2(0, 0, 2)
            copy2(0, 0, 3)
            for g in range(L1G, L2G):
                copy2(0, 0, g)
            square(2)
            read_z1(1)
            with act.Fori(1, NCH // 2 - 1) as i:
                step(i * 2, 0, i)
                step(i * 2 + 1, 1, i)
            step(NCH - 2, 0, NCH // 2 - 1)
            step(NCH - 1, 1, NCH // 2 - 1, more=False)
            rotate_hidden(NCH - 1, x_fine)
            for g in range(4):
                copy2(NCH - 1, 1, g, last=True)
            read_z2(NCH - 2)
            for g in range(4, L2G):
                copy2(NCH - 1, 1, g, last=True)

            def copy_out(g):
                act.wait_ge(turned, g + 1)
                nc.scalar.activation(y_sb[:, g, :].rearrange("p (h k o) -> p h k o", h=2, k=2),
                                     z_out[:, :, :].rearrange("p k (h o) -> p h k o", h=2),
                                     ACT.Copy).then_inc(y_copied, 1)

            for g in range(NCH // GRP - 1):
                copy_out(g)
            read_z2(NCH - 1)
            copy_out(NCH // GRP - 1)


def kernel(r_x, L0_rec_W1, L0_rec_b1, L0_rec_W2, L0_rec_b2):
    import numpy as np
    import concourse.bacc as bacc
    from concourse.bass_utils import run_bass_kernel_spmd

    x, W1, W2 = (np.asarray(a) for a in (r_x, L0_rec_W1, L0_rec_W2))
    W1 = W1.reshape(O1, F, F)
    W2 = W2.reshape(H2, F, H1)
    p = np.arange(P)
    row, upper = p % F, p // F
    coarse = (row[:, None] + 8 * np.arange(NROT)[None, :]) % F
    fine = (row[:, None] + 2 * np.arange(NA)[None, :] + upper[:, None]) % F
    c1 = np.repeat(coarse[:, 1:L1G + 1], NA, axis=1)
    f1 = np.tile(fine, (1, L1G))
    c2 = np.repeat(coarse, NA, axis=1)
    f2 = np.tile(fine, (1, NROT))
    rows = np.arange(F)
    arrays = {
        "xT": np.ascontiguousarray(x.transpose(1, 0, 2).reshape(F, N)),
        "w1f": np.ascontiguousarray(W1[:, f1, c1].transpose(1, 2, 0)).reshape(P, L1G, NA, O1),
        "w1r": np.ascontiguousarray(W1[:, c1, f1].transpose(1, 2, 0)).reshape(P, L1G, NA, O1),
        "w1d": np.ascontiguousarray(W1[:, rows, rows].transpose(1, 0)),
        "w2t": np.ascontiguousarray(W2[:, c2, f2].transpose(1, 2, 0)),
        "b1": np.ascontiguousarray(np.asarray(L0_rec_b1).reshape(O1, 1)),
        "b2": np.ascontiguousarray(np.asarray(L0_rec_b2).reshape(H2, 1)),
    }
    nc = bacc.Bacc("TRN2", target_bir_lowering=False, num_devices=1)
    args = [nc.dram_tensor(name, a.shape, mybir.dt.from_np(a.dtype), kind="ExternalInput").ap()
            for name, a in arrays.items()]
    args.append(nc.dram_tensor("y", (B, O1), mybir.dt.float32, kind="ExternalOutput").ap())
    cin_program(nc, *args)
    return run_bass_kernel_spmd(nc, [arrays], core_ids=[0]).results[0]["y"]
```

```python
import concourse.bass as bass
from concourse import mybir
from contextlib import ExitStack

B, F, E = 1024, 64, 32
H1, H2 = 64, 64
O1 = 2 * H1
N = B * E
CH = 1024
HALF = CH // 2
NCH = N // CH
NB = HALF // E
NA = 4
NROT = 8
L1G = 4
L2G = 8
SLOTS = 4
GRP = 8
SPLIT = (2, 3, 3, 3)
FULL = tuple(NA - n for n in SPLIT)
SPLIT_AT = tuple(sum(SPLIT[:q]) for q in range(L1G))
FULL_AT = tuple(sum(FULL[:q]) for q in range(L1G))
ORDER = (1, 1, 2, 1, 2, 1, 2, 2, 2, 2, 2, 2)
INDEX = tuple(ORDER[:k].count(ORDER[k]) for k in range(len(ORDER)))
PLACE = {(ORDER[k], INDEX[k]): k for k in range(len(ORDER))}
HELPED = (3,)
HELPED_LAST = (0, 1, 2, 3, 6, 7)
READ_Z2 = 1
READ_Z1 = 8
SQUARE = 9
P = 128


def cin_program(nc, xT, w1f, w1r, w1d, w2t, b1, b2, y):
    fp32 = mybir.dt.float32
    fp32r = mybir.dt.float32r
    ALU = mybir.AluOpType
    ACT = mybir.ActivationFunctionType
    AX_X = mybir.AxisListType.X

    ctx = ExitStack()
    with ctx:
        def sb(name, shape, dtype=fp32):
            return ctx.enter_context(nc.sbuf_tensor(name, shape, dtype))

        def sem(name):
            return ctx.enter_context(nc.semaphore(name))

        x_base = sb("x_base", [P, CH])
        x_fine = sb("x_fine", [P, NA, CH])
        x_coarse = sb("x_coarse", [P, 2, L1G, CH])
        x_late = sb("x_late", [P, 2, CH])
        h_base = sb("h_base", [P, CH])
        h_fine = sb("h_fine", [P, NA, CH])
        with nc.sbuf_tensor("prod_low", [P, SLOTS, NA, CH], fp32r) as prod_low:
            pass
        prod = sb("prod", [P, SLOTS, NA, CH])
        prod_hi = sb("prod_hi", [P, 2, max(SPLIT), CH], fp32r)
        squares = sb("squares", [P, CH])
        squares_split = sb("squares_split", [P, CH], fp32r)
        w1 = sb("w1", [P, sum(FULL), O1])
        w1_hi = sb("w1_hi", [P, sum(SPLIT), O1], fp32r)
        w1_lo = sb("w1_lo", [P, sum(SPLIT), O1], fp32r)
        diag_hi = sb("diag_hi", [P, O1], fp32r)
        diag_lo = sb("diag_lo", [F, O1], fp32r)
        w2 = sb("w2", [P, NROT * NA, H2])
        b1_sb = sb("b1_sb", [P, 1])
        b2_sb = sb("b2_sb", [P, 1])
        relus = sb("relus", [P, 2, HALF])
        sums = sb("sums", [P, 2, NCH + 1, NB])
        ident = sb("ident", [P, P])
        w1_swapped = h_fine[:, 0:2, :].rearrange("p a n -> p (a n)").rearrange("p (q a o) -> p q a o", q=L1G, a=NA)
        w1_split = h_fine[:, 2:4, :].rearrange("p a n -> p (a n)").rearrange("p (t o) -> p t o", o=O1)
        diag = sums[:, 0, 0:O1 // NB, :].rearrange("p c b -> p (c b)")
        y_sb = x_coarse[:, 0, 0, :].rearrange("p (g n) -> p g n", g=NCH // GRP)

        coarse_ps = ctx.enter_context(nc.psum_tensor("coarse_ps", [P, 2, CH], fp32))
        z1 = ctx.enter_context(nc.psum_tensor("z1", [P, 2, HALF], fp32))
        z2 = ctx.enter_context(nc.psum_tensor("z2", [P, HALF], fp32))
        z_out = ctx.enter_context(nc.psum_tensor("z_out", [P, 2, P], fp32))

        base_loaded = sem("base_loaded")
        fine_ready = sem("fine_ready")
        first_fine = [sem(f"first_fine{a}") for a in range(NA)]
        coarse_ready = [[sem(f"coarse_ready{s}_{k}") for k in range(L1G)] for s in range(2)]
        late_ready = [sem(f"late_ready{s}") for s in range(2)]
        hfine_ready = sem("hfine_ready")
        coarse1_copied = sem("coarse1_copied")
        coarse2_copied = sem("coarse2_copied")
        hi_made = sem("hi_made")
        lo_made = sem("lo_made")
        w1_loaded = [sem(f"w1_loaded{q}") for q in range(L1G)]
        diag_loaded = sem("diag_loaded")
        w2_loaded = sem("w2_loaded")
        bias_loaded = sem("bias_loaded")
        w1_summed = sem("w1_summed")
        w1_hi_made = sem("w1_hi_made")
        w1_lo_made = sem("w1_lo_made")
        diag_hi_made = sem("diag_hi_made")
        diag_lo_made = sem("diag_lo_made")
        squares_made = sem("squares_made")
        squares_hi_made = sem("squares_hi_made")
        squares_lo_made = sem("squares_lo_made")
        squares_used = sem("squares_used")
        pairs1_made = sem("pairs1_made")
        first_pairs = sem("first_pairs")
        pairs1_used = sem("pairs1_used")
        pairs2_made = sem("pairs2_made")
        pairs2_used = sem("pairs2_used")
        helped_made = sem("helped_made")
        hidden_made = sem("hidden_made")
        z1_read = sem("z1_read")
        z2_read = sem("z2_read")
        reduced = sem("reduced")
        ident_zero = sem("ident_zero")
        ident_made = sem("ident_made")
        turned = sem("turned")
        y_copied = sem("y_copied")
        y_stored = sem("y_stored")

        block = ctx.enter_context(nc.Block())

        def weight_sums(q):
            whole = sum(FULL[k] > (k == L1G - 1) for k in range(q + 1))
            return whole + (q + 1) + q // (L1G - 1)

        def groups1(c, q=L1G - 1):
            return c * L1G + (q + 1)

        def groups2(c, g=L2G - 1):
            return c * L2G + (g + 1)

        def tiles1(c, q=L1G - 1, a=SPLIT[-1] - 1):
            return c * sum(SPLIT) + (SPLIT_AT[q] + a + 1)

        def helped_of(c):
            return HELPED_LAST if isinstance(c, int) and c == NCH - 1 else HELPED

        def helped(c, g=HELPED[-1]):
            return c * len(HELPED) + (helped_of(c).index(g) + 1)

        def before(c, k, slots):
            while True:
                k -= slots
                if k < 0:
                    k, c = k + len(ORDER), c - 1
                if isinstance(c, int) and c < 0:
                    return None
                if isinstance(c, int) and (c == 0 and ORDER[k] == 2 or c == NCH and ORDER[k] == 1):
                    continue
                return ORDER[k], c - (ORDER[k] - 1), INDEX[k]

        def wait_before(engine, c, k, slots, signal1, signal2):
            last = before(c, k, slots)
            if last and last[0] == 1:
                engine.wait_ge(signal1, groups1(last[1], last[2]))
            elif last:
                engine.wait_ge(signal2, groups2(last[1], last[2]))

        @block.sync
        def _(sp):
            def load_base(n0):
                for u in range(2):
                    sp.dma_start(x_base[F * u:F * u + F, :], xT[:, bass.ds(n0, CH)]).then_inc(base_loaded, 16)

            def rotate_fine(ready=(fine_ready,) * NA):
                for a in range(NA):
                    for u in range(2):
                        r = 2 * a + u
                        sp.dma_start(x_fine[F * u:F * u + F, a, :], x_base[r:r + F, :]).then_inc(ready[a], 16)

            def rotate_coarse(s, b):
                for u in range(2):
                    sp.dma_start(x_coarse[F * u:F * u + F, s, b - 1, :],
                                 x_base[8 * b:8 * b + F, :]).then_inc(coarse_ready[s][b - 1], 16)

            def rotate_late(s, m):
                r = 8 * (m + 1)
                for u in range(2):
                    sp.dma_start(x_late[F * u:F * u + F, m % 2, :],
                                 x_coarse[r:r + F, s, L1G - 1, :]).then_inc(late_ready[m % 2], 16)

            regs = []

            def counts(c, s, i):
                def now(v):
                    if isinstance(v, int):
                        return v
                    r = sp.alloc_register(f"count{s}_{len(regs)}")
                    regs.append(r)
                    sp.reg_mov(r, v)
                    return sp.snap(r)

                return {
                    "base": now((c + 1) * 32),
                    "helped": [now(helped(c - 2, g)) for g in HELPED],
                    "read1": now(groups1(c - 1)),
                    "copied": [now(groups2(c - 2, g)) for g in range(2, L2G)],
                    "late": now((c - 1) * 64),
                    "source": now((i + s) * 32),
                    "fine": now(c * 128),
                    "coarse": now(i * 32 + 32),
                    "squared": now(c + 1),
                    "next": (c + 1) * CH,
                }

            def fine_step(n):
                sp.wait_ge(base_loaded, n["base"])
                sp.wait_ge(pairs1_made, n["read1"])
                rotate_fine()

            def late_second(n, s):
                for m in (2, 3):
                    sp.wait_ge(coarse2_copied, n["copied"][L1G + m - 4])
                    rotate_late(s, m)

            def late_first(n, s):
                sp.wait_ge(coarse_ready[1 - s][L1G - 1], n["source"])
                for m in (0, 1):
                    sp.wait_ge(coarse2_copied, n["copied"][L1G + m])
                    rotate_late(1 - s, m)

            def next_base(n, s, first=False):
                if first:
                    for a in range(NA):
                        sp.wait_ge(first_fine[a], 32)
                else:
                    sp.wait_ge(fine_ready, n["fine"])
                for b in range(L1G):
                    sp.wait_ge(coarse_ready[s][b], n["coarse"])
                sp.wait_ge(squares_made, n["squared"])
                load_base(n["next"])

            def wait_helped(n, g):
                if g in HELPED:
                    sp.wait_ge(helped_made, n["helped"][HELPED.index(g)])

            def step(n, s, more=True):
                fine_step(n)
                sp.wait_ge(coarse2_copied, n["copied"][0])
                for b in range(1, L1G):
                    wait_helped(n, b - 1)
                    rotate_coarse(s, b)
                late_second(n, s)
                for m in range(2):
                    sp.wait_ge(late_ready[m], n["late"])
                wait_helped(n, L1G - 1)
                rotate_coarse(s, L1G)
                late_first(n, s)
                if more:
                    next_base(n, s)

            load_base(0)
            sp.wait_ge(base_loaded, 32)
            rotate_coarse(0, 1)
            rotate_fine(ready=first_fine)
            for b in range(2, L1G + 1):
                rotate_coarse(0, b)
            next_base(counts(0, 0, 0), 0, first=True)
            second = counts(1, 1, 0)
            sp.wait_ge(base_loaded, second["base"])
            for b in range(1, L1G + 1):
                rotate_coarse(1, b)
            sp.wait_ge(coarse_ready[0][L1G - 1], second["source"])
            for m in (0, 1):
                rotate_late(0, m)
            fine_step(second)
            next_base(second, 1)
            with sp.Fori(1, NCH // 2 - 1) as i:
                even, odd = counts(i * 2, 0, i), counts(i * 2 + 1, 1, i)
                step(even, 0)
                step(odd, 1)
            step(counts(NCH - 2, 0, NCH // 2 - 1), 0)
            step(counts(NCH - 1, 1, NCH // 2 - 1), 1, more=False)
            beyond = counts(NCH, 0, NCH // 2)
            late_second(beyond, 0)
            late_first(beyond, 0)
            late_second(counts(NCH + 1, 1, NCH // 2), 1)

            y_v = y.rearrange("(g c h b) o -> g h c b o", g=NCH // GRP, c=GRP, h=2)
            for g in range(NCH // GRP):
                sp.wait_ge(y_copied, g + 1)
                for h in range(2):
                    sp.dma_start(y_v[g, h], y_sb[:, g, h * O1:h * O1 + O1]).then_inc(y_stored, 16)
            sp.wait_ge(y_stored, 16 * 2 * (NCH // GRP))

        @block.gpsimd
        def _(pool):
            nc.gpsimd.memset(ident[:], 0.0).then_inc(ident_zero, 1)
            pool.wait_ge(ident_zero, 1)
            nc.gpsimd.affine_select(out=ident[:], in_=ident[:], compare_op=ALU.not_equal, fill=1.0, base=0,
                                    pattern=[[-1, P]], channel_multiplier=1).then_inc(ident_made, 1)

            def squares_rest(c):
                if isinstance(c, int) and c == 0:
                    pool.wait_ge(ident_made, 1)
                else:
                    pool.wait_ge(lo_made, tiles1(c - 1))
                    if not isinstance(c, int) or c > 1:
                        pool.wait_ge(helped_made, helped(c - 2))
                pool.wait_ge(squares_hi_made, c + 1)
                nc.gpsimd.tensor_tensor(squares_split[F:P, :], squares[F:P, :],
                                        squares_split[F:P, :].bitcast(fp32),
                                        ALU.subtract).then_inc(squares_lo_made, 1)

            def rests(c):
                pool.wait_ge(squares_lo_made, c + 1)
                for q in range(L1G):
                    slot = PLACE[1, q] % SLOTS
                    for a in range(SPLIT[q]):
                        pool.wait_ge(hi_made, tiles1(c, q, a))
                        nc.gpsimd.tensor_tensor(prod_low[:, slot, FULL[q] + a], prod[:, slot, FULL[q] + a],
                                                prod_hi[:, q % 2, a].bitcast(fp32), ALU.subtract).then_inc(lo_made, 1)

            def help2(c, s):
                for g in helped_of(c):
                    k = PLACE[2, g]
                    last = isinstance(c, int) and c == NCH - 1
                    pool.wait_ge(hfine_ready, (c + 1) * 128)
                    pool.wait_ge(coarse2_copied, groups2(c, g))
                    wait_before(pool, c + 1, k, SLOTS, pairs1_used, pairs2_used)
                    fine = x_fine if last else h_fine
                    coarse = x_coarse[:, s, g] if g < L1G else x_late[:, g % 2]
                    nc.gpsimd.tensor_tensor(prod[:, k % SLOTS, NA - 1], fine[:, NA - 1], coarse,
                                            ALU.mult).then_inc(helped_made, 1)

            def step(c, s):
                rests(c)
                help2(c - 1, 1 - s)

            squares_rest(0)
            rests(0)
            squares_rest(1)
            step(1, 1)
            squares_rest(2)
            with pool.Fori(1, NCH // 2 - 1) as i:
                step(i * 2, 0)
                squares_rest(i * 2 + 1)
                step(i * 2 + 1, 1)
                squares_rest(i * 2 + 2)
            step(NCH - 2, 0)
            squares_rest(NCH - 1)
            step(NCH - 1, 1)
            help2(NCH - 1, 1)

        @block.vector
        def _(dve):
            def sum_weights(q):
                dve.wait_ge(w1_loaded[q], 48)
                k, n = FULL_AT[q], FULL[q]
                if q == L1G - 1:
                    nc.vector.tensor_tensor(w1[F:P, k, :], w1[F:P, k, :], w1_swapped[F:P, q, 0, :],
                                            ALU.add).then_inc(w1_summed, 1)
                    k, n = k + 1, n - 1
                if n > 0:
                    nc.vector.tensor_tensor(w1[:, k:k + n], w1[:, k:k + n], w1_swapped[:, q, FULL[q] - n:FULL[q], :],
                                            ALU.add).then_inc(w1_summed, 1)
                k, n = SPLIT_AT[q], SPLIT[q]
                nc.vector.tensor_tensor(w1_split[:, k:k + n], w1_split[:, k:k + n], w1_swapped[:, q, FULL[q]:NA, :],
                                        ALU.add).then_inc(w1_summed, 1)

            def split_weights(q):
                dve.wait_ge(w1_hi_made, q + 1)
                k, n = SPLIT_AT[q], SPLIT[q]
                nc.vector.tensor_tensor(w1_lo[:, k:k + n], w1_split[:, k:k + n], w1_hi[:, k:k + n].bitcast(fp32),
                                        ALU.subtract).then_inc(w1_lo_made, 1)

            def copied(slot, n=NA):
                return coarse_ps[:, slot:slot + 1, :].to_broadcast([P, n, CH])

            def group1(c, k):
                q = INDEX[k]
                first = isinstance(c, int) and c == 0
                if q == 0 and not first:
                    dve.wait_ge(fine_ready, c * 128)
                dve.wait_ge(coarse1_copied, groups1(c, q))
                wait_before(dve, c, k, SLOTS, pairs1_used, pairs2_used)
                if first and q == 0:
                    for a in range(NA):
                        dve.wait_ge(first_fine[a], 32)
                        nc.vector.tensor_tensor(prod[:, k % SLOTS, a], x_fine[:, a], coarse_ps[:, k % 2],
                                                ALU.mult).then_inc(pairs1_made if a == NA - 1 else first_pairs, 1)
                else:
                    nc.vector.tensor_tensor(prod[:, k % SLOTS], x_fine[:, :], copied(k % 2),
                                            ALU.mult).then_inc(pairs1_made, 1)
                if first:
                    if q > 0:
                        sum_weights(q)
                    split_weights(q)

            def group2(c, k):
                g = INDEX[k]
                last = isinstance(c, int) and c == NCH - 1
                if g == 0:
                    dve.wait_ge(hfine_ready, (c + 1) * 128)
                dve.wait_ge(coarse2_copied, groups2(c, g))
                wait_before(dve, c + 1, k, SLOTS, pairs1_used, pairs2_used)
                source = x_fine if last else h_fine
                n = NA - (g in helped_of(c))
                nc.vector.tensor_tensor(prod[:, k % SLOTS, 0:n], source[:, 0:n], copied(k % 2, n),
                                        ALU.mult).then_inc(pairs2_made, 1)
                if g == 1 and isinstance(c, int) and c == 0:
                    dve.wait_ge(z1_read, 1)
                    reduce_one(0, 0)
                elif g == 1 and not last:
                    reduce(c)

            def step(c):
                for k, layer in enumerate(ORDER):
                    if layer == 1:
                        group1(c, k)
                    else:
                        group2(c - 1, k)

            def reduce(c):
                dve.wait_ge(z2_read, c)
                nc.vector.reduce_sum(sums[:, :, bass.ds(c, 1), :].rearrange("p k c b -> p k (c b)"),
                                     relus[:, :, :].rearrange("p k (b e) -> p k b e", e=E),
                                     AX_X).then_inc(reduced, 1)

            def reduce_one(c, k):
                nc.vector.reduce_sum(sums[:, k, c, :], relus[:, k, :].rearrange("p (b e) -> p b e", e=E),
                                     AX_X).then_inc(reduced, 1)

            dve.wait_ge(diag_hi_made, 1)
            nc.vector.tensor_tensor(diag_lo[:], diag[0:F, :], diag_hi[0:F, :].bitcast(fp32),
                                    ALU.subtract).then_inc(diag_lo_made, 1)
            sum_weights(0)
            for q in range(L1G):
                group1(0, PLACE[1, q])
            step(1)
            with dve.Fori(1, NCH // 2) as i:
                step(i * 2)
                step(i * 2 + 1)
            for g in range(L2G):
                group2(NCH - 1, PLACE[2, g])
                if g == 1:
                    reduce(NCH - 1)
            dve.wait_ge(z2_read, NCH)
            reduce_one(NCH, 1)

        @block.tensor
        def _(pe):
            pe.wait_ge(diag_lo_made, 1)

            def squares1(c):
                if not isinstance(c, int) or c > 0:
                    pe.wait_ge(z1_read, c)
                pe.wait_ge(squares_lo_made, c + 1)
                for h in range(2):
                    nc.tensor.matmul(z1[:, h, :], diag_hi[:], squares_split[:, h * HALF:(h + 1) * HALF],
                                     start=True, stop=False)
                    mm = nc.tensor.matmul(z1[:, h, :], diag_lo[:], squares_split[0:F, h * HALF:(h + 1) * HALF],
                                          start=False, stop=False)
                mm.then_inc(squares_used, 1)

            def group1(c, k):
                q = INDEX[k]
                first = isinstance(c, int) and c == 0
                if q == 0:
                    squares1(c)
                if first:
                    pe.wait_ge(w1_summed, weight_sums(q))
                if not (first and q == 0):
                    pe.wait_ge(pairs1_made, groups1(c, q))
                for a in range(FULL[q]):
                    if first and q == 0:
                        pe.wait_ge(first_pairs, a + 1)
                    for h in range(2):
                        nc.tensor.matmul(z1[:, h, :], w1[:, FULL_AT[q] + a, :],
                                         prod[:, k % SLOTS, a, h * HALF:(h + 1) * HALF], start=False, stop=False)
                if first:
                    pe.wait_ge(w1_lo_made, q + 1)
                for a in range(SPLIT[q]):
                    pe.wait_ge(lo_made, tiles1(c, q, a))
                    high = prod_hi[:, q % 2, a]
                    low = prod_low[:, k % SLOTS, FULL[q] + a]
                    for h in range(2):
                        for w, p in ((w1_hi, high), (w1_lo, high), (w1_hi, low)):
                            mm = nc.tensor.matmul(z1[:, h, :], w[:, SPLIT_AT[q] + a, :],
                                                  p[:, h * HALF:(h + 1) * HALF], start=False,
                                                  stop=(q == L1G - 1 and a == SPLIT[q] - 1 and p is low))
                mm.then_inc(pairs1_used, 1)

            def group2(c, k):
                g = INDEX[k]
                b = (g + 1) % NROT
                if g == 0 and not (isinstance(c, int) and c == 0):
                    pe.wait_ge(z2_read, c)
                pe.wait_ge(pairs2_made, groups2(c, g))
                for a in range(NA):
                    if a == NA - 1 and g in helped_of(c):
                        pe.wait_ge(helped_made, helped(c, g))
                    for h in range(2):
                        mm = nc.tensor.matmul(z2[F * h:F * h + F, :], w2[:, NA * b + a, :],
                                              prod[:, k % SLOTS, a, h * HALF:(h + 1) * HALF],
                                              start=(g == 0 and a == 0), stop=(g == L2G - 1 and a == NA - 1))
                mm.then_inc(pairs2_used, 1)

            def step(c):
                for k, layer in enumerate(ORDER):
                    if layer == 1:
                        group1(c, k)
                    else:
                        group2(c - 1, k)

            pe.wait_ge(ident_made, 1)

            def turn(g):
                pe.wait_ge(reduced, GRP * (g + 1) + 1)
                if g >= 1:
                    pe.wait_ge(y_copied, g)
                for k in range(2):
                    mm = nc.tensor.transpose(z_out[:, k, :],
                                             sums[:, k, GRP * g + k:GRP * g + k + GRP, :].rearrange("p c b -> p (c b)"),
                                             ident[:])
                mm.then_inc(turned, 1)

            for q in range(L1G):
                group1(0, PLACE[1, q])
            pe.wait_ge(w2_loaded, 16)
            step(1)
            with pe.Fori(1, NCH // 2) as i:
                step(i * 2)
                step(i * 2 + 1)
            for g in range(NCH // GRP - 1):
                turn(g)
            for g in range(L2G):
                group2(NCH - 1, PLACE[2, g])
            turn(NCH // GRP - 1)

        @block.scalar
        def _(act):
            def load_w1(q):
                act.dma_start(w1[:, FULL_AT[q]:FULL_AT[q] + FULL[q]],
                              w1f[:, q, 0:FULL[q], :]).then_inc(w1_loaded[q], 16)
                act.dma_start(w1_split[:, SPLIT_AT[q]:SPLIT_AT[q] + SPLIT[q]],
                              w1f[:, q, FULL[q]:NA, :]).then_inc(w1_loaded[q], 16)
                act.dma_start(w1_swapped[:, q], w1r[:, q]).then_inc(w1_loaded[q], 16)

            def round_w1(q):
                act.wait_ge(w1_summed, weight_sums(q))
                k, n = SPLIT_AT[q], SPLIT[q]
                nc.scalar.activation(w1_hi[:, k:k + n], w1_split[:, k:k + n], ACT.Copy).then_inc(w1_hi_made, 1)

            load_w1(0)
            for h in range(2):
                act.dma_start(diag[F * h:F * h + F, :], w1d).then_inc(diag_loaded, 16)
            act.dma_start(b1_sb[:], b1).then_inc(bias_loaded, 16)
            for h in range(2):
                act.dma_start(b2_sb[F * h:F * h + F, :], b2).then_inc(bias_loaded, 16)

            def square(c):
                act.wait_ge(base_loaded, (c + 1) * 32)
                if not isinstance(c, int) or c > 0:
                    act.wait_ge(squares_used, c)
                nc.scalar.activation(squares[:], x_base[:], ACT.Square).then_inc(squares_made, 1)
                act.wait_ge(squares_made, c + 1)
                nc.scalar.activation(squares_split[:], squares[:], ACT.Copy).then_inc(squares_hi_made, 1)

            def copy1(c, s, i, k):
                q = INDEX[k]
                act.wait_ge(coarse_ready[s][q], i * 32 + 32)
                wait_before(act, c, k, 2, pairs1_made, pairs2_made)
                nc.scalar.activation(coarse_ps[:, k % 2, :], x_coarse[:, s, q, :],
                                     ACT.Copy).then_inc(coarse1_copied, 1)

            def copy2(c, s, k):
                g = INDEX[k]
                m = g - L1G
                if m >= 0:
                    act.wait_ge(late_ready[m % 2], c * 64 + 32 * (m // 2 + 1))
                wait_before(act, c + 1, k, 2, pairs1_made, pairs2_made)
                source = x_coarse[:, s, g, :] if m < 0 else x_late[:, m % 2, :]
                nc.scalar.activation(coarse_ps[:, k % 2, :], source, ACT.Copy).then_inc(coarse2_copied, 1)

            def round_high(c, q):
                act.wait_ge(pairs1_made, groups1(c, q))
                if q >= 2:
                    act.wait_ge(pairs1_used, groups1(c, q - 2))
                elif not isinstance(c, int) or c > 0:
                    act.wait_ge(pairs1_used, groups1(c - 1, q + 2))
                for a in range(SPLIT[q]):
                    nc.scalar.activation(prod_hi[:, q % 2, a], prod[:, PLACE[1, q] % SLOTS, FULL[q] + a],
                                         ACT.Copy).then_inc(hi_made, 1)

            def read_z1(c):
                act.wait_ge(pairs1_used, groups1(c))
                if not isinstance(c, int) or c > 0:
                    act.wait_ge(hfine_ready, c * 128)
                z1_rows = z1[H1:O1].rearrange("p h n -> p (h n)")
                for h in range(2):
                    nc.scalar.activation(h_base[F * h:F * h + F, :], z1_rows, ACT.Relu,
                                         bias=b1_sb[H1:O1, :]).then_inc(hidden_made, 1)
                if not isinstance(c, int) or c > 0:
                    act.wait_ge(reduced, c)
                for h in range(2):
                    rd = nc.scalar.activation(relus[F * h:F * h + F, 0, :], z1[0:H1, h, :], ACT.Relu,
                                              bias=b1_sb[0:H1, :])
                rd.then_inc(z1_read, 1)

            def rotate_hidden(c, to):
                act.wait_ge(hidden_made, c * 2 + 2)
                if isinstance(c, int) and c == NCH - 1:
                    act.wait_ge(pairs1_made, groups1(c))
                elif not isinstance(c, int) or c > 0:
                    act.wait_ge(pairs2_made, groups2(c - 1))
                    act.wait_ge(helped_made, helped(c - 1))
                else:
                    act.wait_ge(w1_lo_made, L1G)
                for r in range(2 * NA):
                    a, u = r // 2, r % 2
                    act.dma_start(to[F * u:F * u + F, a, :], h_base[r:r + F, :]).then_inc(hfine_ready, 16)

            def read_z2(c):
                act.wait_ge(pairs2_used, groups2(c))
                if not isinstance(c, int) or c > 0:
                    act.wait_ge(reduced, c + 1)
                nc.scalar.activation(relus[:, 1, :], z2[:, :], ACT.Relu, bias=b2_sb[:]).then_inc(z2_read, 1)

            def copy(c, s, i, k):
                if ORDER[k] == 1:
                    copy1(c, s, i, k)
                else:
                    copy2(c - 1, 1 - s, k)

            def step(c, s, i, more=True):
                copy(c, s, i, 0)
                copy(c, s, i, 1)
                if isinstance(c, int) and c == 1:
                    read_z1(0)
                rotate_hidden(c - 1, h_fine)
                for k in range(len(ORDER)):
                    if ORDER[k] == 1:
                        round_high(c, INDEX[k])
                    if k + 2 < len(ORDER):
                        copy(c, s, i, k + 2)
                    if k == READ_Z2 and (not isinstance(c, int) or c > 1):
                        read_z2(c - 2)
                    if k == READ_Z1:
                        read_z1(c)
                    if k == SQUARE and more:
                        square(c + 1)

            copy1(0, 0, 0, 0)
            square(0)
            act.wait_ge(diag_loaded, 32)
            nc.scalar.activation(diag_hi[:], diag, ACT.Copy).then_inc(diag_hi_made, 1)
            round_w1(0)
            act.wait_ge(first_fine[0], 32)
            load_w1(1)
            act.wait_ge(first_fine[NA - 1], 32)
            load_w1(2)
            load_w1(3)
            copy1(0, 0, 0, PLACE[1, 1])
            for q in range(L1G):
                if q > 0:
                    round_w1(q)
                round_high(0, q)
                if q + 2 < L1G:
                    copy1(0, 0, 0, PLACE[1, q + 2])
            square(1)
            act.wait_ge(bias_loaded, 48)
            act.dma_start(w2[:], w2t).then_inc(w2_loaded, 16)
            step(1, 1, 0)
            with act.Fori(1, NCH // 2 - 1) as i:
                step(i * 2, 0, i)
                step(i * 2 + 1, 1, i)
            step(NCH - 2, 0, NCH // 2 - 1)
            step(NCH - 1, 1, NCH // 2 - 1, more=False)
            rotate_hidden(NCH - 1, x_fine)
            def copy_out(g):
                act.wait_ge(turned, g + 1)
                nc.scalar.activation(y_sb[:, g, :].rearrange("p (h k o) -> p h k o", h=2, k=2),
                                     z_out[:, :, :].rearrange("p k (h o) -> p h k o", h=2),
                                     ACT.Copy).then_inc(y_copied, 1)

            for g in range(2):
                copy2(NCH - 1, 1, PLACE[2, g])
            read_z2(NCH - 2)
            for g in range(NCH // GRP - 1):
                copy_out(g)
            for g in range(2, L2G):
                copy2(NCH - 1, 1, PLACE[2, g])
            read_z2(NCH - 1)
            copy_out(NCH // GRP - 1)


def kernel(r_x, L0_rec_W1, L0_rec_b1, L0_rec_W2, L0_rec_b2):
    import numpy as np
    import concourse.bacc as bacc
    from concourse.bass_utils import run_bass_kernel_spmd

    x, W1, W2 = (np.asarray(a) for a in (r_x, L0_rec_W1, L0_rec_W2))
    W1 = W1.reshape(O1, F, F)
    W2 = W2.reshape(H2, F, H1)
    p = np.arange(P)
    row, upper = p % F, p // F
    coarse = (row[:, None] + 8 * np.arange(NROT)[None, :]) % F
    fine = (row[:, None] + 2 * np.arange(NA)[None, :] + upper[:, None]) % F
    c1 = np.repeat(coarse[:, 1:L1G + 1], NA, axis=1)
    f1 = np.tile(fine, (1, L1G))
    c2 = np.repeat(coarse, NA, axis=1)
    f2 = np.tile(fine, (1, NROT))
    rows = np.arange(F)
    arrays = {
        "xT": np.ascontiguousarray(x.transpose(1, 0, 2).reshape(F, N)),
        "w1f": np.ascontiguousarray(W1[:, f1, c1].transpose(1, 2, 0)).reshape(P, L1G, NA, O1),
        "w1r": np.ascontiguousarray(W1[:, c1, f1].transpose(1, 2, 0)).reshape(P, L1G, NA, O1),
        "w1d": np.ascontiguousarray(W1[:, rows, rows].transpose(1, 0)),
        "w2t": np.ascontiguousarray(W2[:, c2, f2].transpose(1, 2, 0)),
        "b1": np.ascontiguousarray(np.asarray(L0_rec_b1).reshape(O1, 1)),
        "b2": np.ascontiguousarray(np.asarray(L0_rec_b2).reshape(H2, 1)),
    }
    nc = bacc.Bacc("TRN2", target_bir_lowering=False, num_devices=1)
    args = [nc.dram_tensor(name, a.shape, mybir.dt.from_np(a.dtype), kind="ExternalInput").ap()
            for name, a in arrays.items()]
    args.append(nc.dram_tensor("y", (B, O1), mybir.dt.float32, kind="ExternalOutput").ap())
    cin_program(nc, *args)
    return run_bass_kernel_spmd(nc, [arrays], core_ids=[0]).results[0]["y"]
```
